# Optimizing a Trainium2 kernel written in Bass

```python
import numpy as np
import jax
import jax.numpy as jnp

def _softmax(x, axis=-1):
    return jax.nn.softmax(x, axis=axis)

def _gelu(x):
    return jax.nn.gelu(x, approximate=True)

def _silu(x):
    return jax.nn.silu(x)

def _sigmoid(x):
    return jax.nn.sigmoid(x)

def _layernorm(x, axis=-1, eps=1e-05):
    m = jnp.mean(x, axis=axis, keepdims=True)
    v = jnp.var(x, axis=axis, keepdims=True)
    return (x - m) / jnp.sqrt(v + eps)

def _scatter_add(tgt, idx, src, axis=0):
    return tgt.at[idx].add(src)

def _segment_sum(src, seg, n):
    return jax.ops.segment_sum(src, seg, n)
kernel_name = 'mk_adj_resnorm_d1_adj_r2_a13a8f'

def setup_inputs(seed: int=0):
    np.random.seed(seed)
    _w = jnp.asarray

    def _rec_inputs():
        import jax
        import jax.numpy as jnp
        _gk = jax.random.key(seed)
        x = -0.0001538 + 1 * jax.random.normal(jax.random.fold_in(_gk, 1), (128, 128, 384), jnp.float32)
        _a = jax.random.bernoulli(jax.random.fold_in(_gk, 2), 0.0625, (128, 128, 128))
        _a = jnp.logical_or(_a, jnp.swapaxes(_a, -1, -2))
        _a = jnp.logical_or(_a, jnp.eye(128, dtype=bool))
        _af = _a.astype(jnp.float32)
        _af = _af * jax.random.uniform(jax.random.fold_in(_gk, 3), (128, 128, 128), jnp.float32, 0.05, 4.42607)
        adj = _af
        return (x, adj)
    x, adj = _rec_inputs()

    def _L0_gnn_setup():
        import jax, jax.numpy as jnp
        import numpy as np
        NUM_HEADS = 12
        HIDDEN = 384
        HEAD = HIDDEN // NUM_HEADS
        SCALE = HIDDEN ** (-0.5)
        key = jax.random.key(seed)
        ks = jax.random.split(key, 8)
        B, N = (16, 256)
        std = HIDDEN ** (-0.5)
        return {'x': jax.random.normal(ks[0], (B, N, HIDDEN), dtype=jnp.float32), 'encoding_bias': jax.random.normal(ks[1], (B, N, N), dtype=jnp.float32), 'Wq': jax.random.normal(ks[2], (HIDDEN, HIDDEN), dtype=jnp.float32) * std, 'Wk': jax.random.normal(ks[3], (HIDDEN, HIDDEN), dtype=jnp.float32) * std, 'Wv': jax.random.normal(ks[4], (HIDDEN, HIDDEN), dtype=jnp.float32) * std, 'bv': jax.random.normal(ks[5], (HIDDEN,), dtype=jnp.float32) * 0.01, 'Wo': jax.random.normal(ks[6], (HIDDEN, HIDDEN), dtype=jnp.float32) * std, 'bo': jax.random.normal(ks[7], (HIDDEN,), dtype=jnp.float32) * 0.01}
    _L0_gnn_all = _L0_gnn_setup()
    _L0_gnn_in = {k: v for k, v in _L0_gnn_all.items() if k in ('Wq', 'Wk', 'Wv', 'bv', 'Wo', 'bo')}
    del _L0_gnn_all
    return {'x': x, 'adj': adj, 'L0_gnn_Wq': _L0_gnn_in['Wq'], 'L0_gnn_Wk': _L0_gnn_in['Wk'], 'L0_gnn_Wv': _L0_gnn_in['Wv'], 'L0_gnn_bv': _L0_gnn_in['bv'], 'L0_gnn_Wo': _L0_gnn_in['Wo'], 'L0_gnn_bo': _L0_gnn_in['bo']}

def reference(x, adj, L0_gnn_Wq, L0_gnn_Wk, L0_gnn_Wv, L0_gnn_bv, L0_gnn_Wo, L0_gnn_bo):
    import jax
    import jax.numpy as jnp

    def _L0_gnn_ref(x, encoding_bias, Wq, Wk, Wv, bv, Wo, bo):
        import jax, jax.numpy as jnp
        import numpy as np
        NUM_HEADS = 12
        HIDDEN = 384
        HEAD = HIDDEN // NUM_HEADS
        SCALE = HIDDEN ** (-0.5)
        B, N, _ = x.shape
        q = (x @ Wq.T).reshape(B, N, NUM_HEADS, HEAD)
        k = (x @ Wk.T).reshape(B, N, NUM_HEADS, HEAD)
        v = (x @ Wv.T + bv).reshape(B, N, NUM_HEADS, HEAD)
        a = jnp.einsum('bnhd,bmhd->bhnm', q, k) * SCALE + encoding_bias[:, None, :, :]
        pad_mask = jnp.all(a == 0, axis=-1)
        a = jnp.where(pad_mask[..., None], -jnp.inf, a)
        a = jax.nn.softmax(a, axis=-1)
        a = jnp.nan_to_num(a)
        o = jnp.einsum('bhnm,bmhd->bnhd', a, v).reshape(B, N, HIDDEN)
        return o @ Wo.T + bo
    x = _layernorm(x + _L0_gnn_ref(x, adj, L0_gnn_Wq, L0_gnn_Wk, L0_gnn_Wv, L0_gnn_bv, L0_gnn_Wo, L0_gnn_bo), axis=-1)
    return x

_drawn_inputs = setup_inputs


def setup_inputs(seed=0):
    import zlib

    import numpy as np

    out = dict(_drawn_inputs(seed))
    spreads = {}
    factors = {'L0_gnn_bv': 5.273, 'L0_gnn_bo': 5.82}
    for name, (base, spread) in spreads.items():
        noise = np.random.default_rng([zlib.crc32(name.encode()), seed]).standard_normal(out[name].shape)
        drawn = base * np.exp(spread * noise) if base else spread * noise
        out[name] = jnp.asarray(drawn.astype(out[name].dtype))
    for name, factor in factors.items():
        out[name] = (out[name] * factor).astype(out[name].dtype)
    return out
```

```python
import concourse.bass as bass
from concourse import mybir
from contextlib import ExitStack

BATCH, N, HIDDEN, HEADS = 128, 128, 384, 12
HEAD = HIDDEN // HEADS
P = 128
CHUNKS = HIDDEN // P
ROWS = P // HEAD
QUAD = 4
QUADS = BATCH // QUAD
TOK = QUAD * N
QK = 2 * CHUNKS
HALF = HEADS // 2
SCALE = float(HIDDEN) ** -0.5
EPS = 1e-5
BIG = 3.0e38
LN_STEPS = 4
MASK_STEPS = 6


def attention_kernel(nc, x, adj, wq_t, wk_t, wv_t, wo_t, bv, bo, out):
    f32 = mybir.dt.float32
    f32r = mybir.dt.float32r
    ACT = mybir.ActivationFunctionType
    ALU = mybir.AluOpType
    AX = mybir.AxisListType

    ctx = ExitStack()
    with ctx:
        def sb(name, shape, dt=f32):
            return ctx.enter_context(nc.sbuf_tensor(name, shape, dt))

        def bank(name):
            return ctx.enter_context(nc.psum_tensor(name, [P, 512], f32))

        def sem(name):
            return ctx.enter_context(nc.semaphore(name))

        x_sb = [sb(f"x_sb{p}", [P, QUAD, HIDDEN]) for p in range(2)]
        xb_sb = [sb(f"xb_sb{p}", [P, QUAD, HIDDEN]) for p in range(2)]
        adj_sb = [sb(f"adj_sb{p}", [P, QUAD, N]) for p in range(2)]
        xT_hi = sb("xT_hi", [P, CHUNKS, TOK], f32r)
        xT_lo = sb("xT_lo", [P, CHUNKS, TOK], f32r)
        qkT = [sb(f"qkT{p}", [P, QK, TOK]) for p in range(2)]
        v_sb = [sb(f"v_sb{p}", [P, QUAD, HIDDEN]) for p in range(2)]
        neg_a = [sb(f"neg_a{p}", [P, HEADS, N]) for p in range(2)]
        neg_max = [sb(f"neg_max{p}", [P, HEADS]) for p in range(2)]
        row_sum = [sb(f"row_sum{p}", [P, HEADS]) for p in range(2)]
        probs = [sb(f"probs{p}", [P, HEADS, N]) for p in range(2)]
        fold = sb("fold", [P, HEADS, N // 2])
        neg_sum = sb("neg_sum", [P, HEADS])
        live = sb("live", [P, HEADS])
        inv_sum = sb("inv_sum", [P, HEADS])
        row_scale = sb("row_scale", [P, HEADS])
        pT = sb("pT", [P, HEADS, N])
        oT_hi = sb("oT_hi", [P, CHUNKS, N], f32r)
        oT_lo = sb("oT_lo", [P, CHUNKS, N], f32r)
        y_sb = sb("y_sb", [P, HIDDEN])
        stats = sb("stats", [P, 6])
        mean_var = sb("mean_var", [P, 2])
        var_eps = sb("var_eps", [P, 1])
        minus_half = sb("minus_half", [P, 1])
        inv_std = sb("inv_std", [P, 1])
        out_sb = sb("out_sb", [P, QUAD, HIDDEN])
        w_raw = sb("w_raw", [P, CHUNKS, 4 * HIDDEN])
        w_hi = sb("w_hi", [P, CHUNKS, 4 * HIDDEN], f32r)
        w_lo = sb("w_lo", [P, CHUNKS, 4 * HIDDEN], f32r)
        bv_sb = sb("bv_sb", [P, HIDDEN])
        bo_sb = sb("bo_sb", [P, HIDDEN])
        ident = sb("ident", [P, P])

        score_bank = [bank(f"score_bank{i}") for i in range(2)]
        pT_bank = [bank(f"pT_bank{i}") for i in range(2)]
        proj_bank = [bank(f"proj_bank{i}") for i in range(2)]
        oT_bank = bank("oT_bank")
        y_bank = bank("y_bank")

        w_loaded, b_loaded = sem("w_loaded"), sem("b_loaded")
        x_loaded = [sem(f"x_loaded{p}") for p in range(2)]
        adj_loaded = [sem(f"adj_loaded{p}") for p in range(2)]
        out_stored = [sem(f"out_stored{b}") for b in range(QUAD)]
        ident_steps = sem("ident_steps")
        w_prep, w_steps = sem("w_prep"), sem("w_steps")
        xT_psum = sem("xT_psum")
        xT_hi_done = sem("xT_hi_done")
        xT_lo_done = sem("xT_lo_done")
        qk_psum = sem("qk_psum")
        qk_done = sem("qk_done")
        v_psum = sem("v_psum")
        v_done = sem("v_done")
        scores_psum = sem("scores_psum")
        neg_a_done = sem("neg_a_done")
        exp_done = sem("exp_done")
        fold_done = sem("fold_done")
        mask_steps = sem("mask_steps")
        scale_done = sem("scale_done")
        probs_done = sem("probs_done")
        pT_psum = sem("pT_psum")
        pT_done = sem("pT_done")
        oT_psum = sem("oT_psum")
        oT_hi_done = sem("oT_hi_done")
        oT_lo_done = sem("oT_lo_done")
        y_psum = sem("y_psum")
        ln_steps = sem("ln_steps")
        inv_std_done = sem("inv_std_done")
        out_done = sem("out_done")
        xb_done = sem("xb_done")

        block = ctx.enter_context(nc.Block())

        def ahead(j, p, n):
            return j + (p + n) // 2, (p + n) % 2

        def next_graph(j, p, b):
            return (j, p, b + 1) if b + 1 < QUAD else (*ahead(j, p, 1), 0)

        def over_quads(eng, quad):
            with eng.Fori(0, QUADS // 2 - 1) as j:
                for p in range(2):
                    quad(j, p, True, True)
            for p in range(2):
                quad(QUADS // 2 - 1, p, p == 0, False)

        @block.sync
        def _(sp):
            for b in range(QUAD):
                sp.sem_inc(out_stored[b], 16)

            def load_x(graph, p):
                sp.dma_start(x_sb[p][:, :, :], x[bass.ds(graph, QUAD), :, :]
                             .rearrange("b n f -> n b f")).then_inc(x_loaded[p], 16)

            def load_adj(graph, p):
                sp.dma_start(adj_sb[p][:, :, :], adj[bass.ds(graph, QUAD), :, :]
                             .rearrange("b n m -> n b m")).then_inc(adj_loaded[p], 16)

            load_x(0, 0)
            for i, w in enumerate((wq_t, wk_t, wv_t, wo_t)):
                sp.dma_start(w_raw[:, :, i * HIDDEN:(i + 1) * HIDDEN],
                             w.rearrange("(c p) o -> p c o", p=P)).then_inc(w_loaded, 16)
            load_x(QUAD, 1)
            load_adj(0, 0)
            for vec, tile in ((bv, bv_sb), (bo, bo_sb)):
                sp.dma_start(tile[:, :], vec.rearrange("(a f) -> a f", a=1).broadcast_to([P, HIDDEN]))\
                  .then_inc(b_loaded, 16)

            def quad(j, p, has_next, has_after):
                q = 2 * j + p
                for value in (q + 1, *(QUAD * q + n for n in range(2 * QUAD + 1)), 16 * q + 1):
                    sp.compute_val(value)
                if has_after:
                    sp.wait_ge(xT_psum, QUAD * q + QUAD)
                    sp.wait_ge(xb_done, q + 1)
                    load_x(QUAD * q + 2 * QUAD, p)
                if has_next:
                    sp.wait_ge(neg_a_done, 16 * q + 1)
                    load_adj(QUAD * q + QUAD, 1 - p)
                for b in range(QUAD):
                    sp.wait_ge(out_done, QUAD * q + b + 1)
                    sp.dma_start(out[bass.ds(QUAD * q + b, 1), :, :].rearrange("b n f -> n (b f)"),
                                 out_sb[:, b, :]).then_inc(out_stored[b], 16)

            over_quads(sp, quad)
            for b in range(QUAD):
                sp.wait_ge(out_stored[b], 16 * (QUADS + 1))

        @block.tensor
        def _(pe):
            def split_product(dst, stat_hi, stat_lo, mov_hi, mov_lo):
                for c in range(CHUNKS):
                    nc.tensor.matmul(dst, stat_hi(c), mov_hi(c), start=(c == 0), stop=False)
                    nc.tensor.matmul(dst, stat_hi(c), mov_lo(c), start=False, stop=False)
                    last = nc.tensor.matmul(dst, stat_lo(c), mov_hi(c), start=False, stop=(c == CHUNKS - 1))
                return last

            def transpose_x(j, p, b):
                q = 2 * j + p
                if b == 0:
                    pe.wait_ge(x_loaded[p], 16 * (j + 1))
                if b >= 2:
                    pe.wait_ge(xT_lo_done, QUAD * q + b - 1)
                elif not (isinstance(q, int) and q == 0):
                    pe.wait_ge(v_done, QUAD * q + b - 1)
                for c in range(CHUNKS):
                    last = nc.tensor.transpose(proj_bank[b % 2][:, c * P:(c + 1) * P],
                                               x_sb[p][:, b, c * P:(c + 1) * P], ident[:, :])
                last.then_inc(xT_psum, 1)

            def project_qk(j, p, k):
                q = 2 * j + p
                if k == 0:
                    pe.wait_ge(xT_lo_done, QUAD * q + QUAD)
                if k in (2, 4):
                    pe.wait_ge(qk_done, QK * q + k)
                elif k in (3, 5):
                    pe.wait_ge(v_done, QUAD * q + (k - 1) // 2)
                split_product(proj_bank[QK_BANK[k]][:, :],
                              lambda c: w_hi[:, c, k * P:(k + 1) * P], lambda c: w_lo[:, c, k * P:(k + 1) * P],
                              lambda c: xT_hi[:, c, :], lambda c: xT_lo[:, c, :]).then_inc(qk_psum, 1)

            def project_v(j, p, b):
                q = 2 * j + p
                pe.wait_ge(qk_done, QK * q + (1, 3, 5, 6)[b])
                tok = slice(b * N, (b + 1) * N)
                split_product(proj_bank[V_BANK[b]][:, 0:HIDDEN],
                              lambda c: xT_hi[:, c, tok], lambda c: xT_lo[:, c, tok],
                              lambda c: w_hi[:, c, 2 * HIDDEN:3 * HIDDEN],
                              lambda c: w_lo[:, c, 2 * HIDDEN:3 * HIDDEN]).then_inc(v_psum, 1)

            def scores(j, p, b, pair):
                t = QUAD * (2 * j + p) + b
                if b == 0 and pair == 0:
                    pe.wait_ge(qk_done, QK * (2 * j + p) + QK)
                if pair == 1 or not (isinstance(t, int) and t == 0):
                    pe.wait_ge(neg_a_done, 4 * t + 2 * pair)
                tok = slice(b * N, (b + 1) * N)
                for c in range(CHUNKS):
                    for r in range(2):
                        row = slice(HEAD * (2 * pair + r), HEAD * (2 * pair + r + 1))
                        last = nc.tensor.matmul(score_bank[r][:, c * N:(c + 1) * N], qkT[p][row, c, tok],
                                                qkT[p][row, CHUNKS + c, tok], start=True, stop=True)
                        if c == CHUNKS - 1:
                            last.then_inc(scores_psum, 1)

            def transpose_probs(j, p, b, pair):
                t = QUAD * (2 * j + p) + b
                pe.wait_ge(probs_done, 2 * t + pair + 1)
                for r in range(2):
                    trio = 2 * pair + r
                    if pair == 1:
                        pe.wait_ge(pT_done, 4 * t + r + 1)
                    for c in range(CHUNKS):
                        last = nc.tensor.transpose(pT_bank[r][:, c * N:(c + 1) * N],
                                                   probs[b % 2][:, 3 * trio + c, :], ident[:, :])
                    last.then_inc(pT_psum, 1)

            def attend(j, p, b):
                t = QUAD * (2 * j + p) + b
                if b == 0:
                    pe.wait_ge(v_done, t + QUAD)
                pe.wait_ge(pT_done, 4 * t + 4)
                for c in range(CHUNKS):
                    for r in range(ROWS):
                        h = ROWS * c + r
                        last = nc.tensor.matmul(oT_bank[HEAD * r:HEAD * (r + 1), c * N:(c + 1) * N],
                                                v_sb[p][:, b, HEAD * h:HEAD * (h + 1)],
                                                pT[:, CHUNKS * r + c, :], start=True, stop=True)
                last.then_inc(oT_psum, 1)

            def project_out(j, p, b):
                t = QUAD * (2 * j + p) + b
                pe.wait_ge(oT_lo_done, t + 1)
                split_product(y_bank[:, 0:HIDDEN],
                              lambda c: oT_hi[:, c, :], lambda c: oT_lo[:, c, :],
                              lambda c: w_hi[:, c, 3 * HIDDEN:4 * HIDDEN],
                              lambda c: w_lo[:, c, 3 * HIDDEN:4 * HIDDEN]).then_inc(y_psum, 1)

            def graph(j, p, b, has_next, has_after):
                nxt, aft = ahead(j, p, 1), ahead(j, p, 2)
                more = b + 1 < QUAD or has_next
                if more:
                    scores(*next_graph(j, p, b), 0)
                if has_next:
                    if b < 2:
                        project_qk(*nxt, 2 * b)
                    if b == 3:
                        project_v(*nxt, 2)
                transpose_probs(j, p, b, 0)
                if more:
                    scores(*next_graph(j, p, b), 1)
                transpose_probs(j, p, b, 1)
                if has_next:
                    if b < 2:
                        project_qk(*nxt, 2 * b + 1)
                    if b == 2:
                        project_qk(*nxt, 4)
                    if b == 3:
                        project_v(*nxt, 3)
                attend(j, p, b)
                if has_next:
                    if b < 2:
                        project_v(*nxt, b)
                    if b == 2:
                        project_qk(*nxt, 5)
                if has_after and b == 3:
                    transpose_x(*aft, 0)
                    transpose_x(*aft, 1)
                project_out(j, p, b)
                if has_after and b == 3:
                    transpose_x(*aft, 2)
                    transpose_x(*aft, 3)

            def quad(j, p, has_next, has_after):
                for b in range(QUAD):
                    graph(j, p, b, has_next, has_after)

            pe.wait_ge(ident_steps, 2)
            for b in range(QUAD):
                transpose_x(0, 0, b)
            pe.wait_ge(w_steps, 1)
            for k, b in ((0, None), (1, 0), (2, None), (3, 1), (4, None), (5, 2)):
                project_qk(0, 0, k)
                if b is not None:
                    project_v(0, 0, b)
            project_v(0, 0, 3)
            for b in range(QUAD):
                transpose_x(0, 1, b)
            scores(0, 0, 0, 0)
            scores(0, 0, 0, 1)
            over_quads(pe, quad)

        @block.scalar
        def _(act):
            def keep_xT_hi(j, p, b):
                act.wait_ge(xT_psum, QUAD * (2 * j + p) + b + 1)
                nc.scalar.activation(xT_hi[:, :, b * N:(b + 1) * N],
                                     proj_bank[b % 2][:, 0:HIDDEN].rearrange("p (c n) -> p c n", c=CHUNKS),
                                     ACT.Copy).then_inc(xT_hi_done, 1)

            def keep_qk(j, p, k):
                act.wait_ge(qk_psum, QK * (2 * j + p) + k + 1)
                nc.scalar.activation(qkT[p][:, k, :], proj_bank[QK_BANK[k]][:, :], ACT.Copy)\
                    .then_inc(qk_done, 1)

            def exp_trio(j, p, b, trio):
                act.wait_ge(neg_a_done, 4 * (QUAD * (2 * j + p) + b) + trio + 1)
                for u in range(CHUNKS * trio, CHUNKS * (trio + 1)):
                    last = nc.scalar.activation(probs[b % 2][:, u, :], neg_a[b % 2][:, u, :], ACT.Exp,
                                                bias=neg_max[b % 2][:, u:u + 1], scale=-1.0,
                                                accum_out=row_sum[b % 2][:, u:u + 1])
                last.then_inc(exp_done, 1)

            def keep_pT(j, p, b, trio):
                act.wait_ge(pT_psum, 4 * (QUAD * (2 * j + p) + b) + trio + 1)
                nc.scalar.activation(pT[:, CHUNKS * trio:CHUNKS * (trio + 1), :],
                                     pT_bank[trio % 2][:, 0:HIDDEN].rearrange("p (c n) -> p c n", c=CHUNKS),
                                     ACT.Copy).then_inc(pT_done, 1)

            def keep_oT_hi(j, p, b):
                act.wait_ge(oT_psum, QUAD * (2 * j + p) + b + 1)
                nc.scalar.activation(oT_hi[:, :, :],
                                     oT_bank[:, 0:HIDDEN].rearrange("p (c n) -> p c n", c=CHUNKS),
                                     ACT.Copy).then_inc(oT_hi_done, 1)

            def graph(j, p, b, has_next, has_after):
                nxt, aft = ahead(j, p, 1), ahead(j, p, 2)
                more = b + 1 < QUAD or has_next
                if more:
                    exp_trio(*next_graph(j, p, b), 0)
                if has_next and b < 2:
                    keep_qk(*nxt, 2 * b)
                keep_pT(j, p, b, 0)
                keep_pT(j, p, b, 1)
                if more:
                    exp_trio(*next_graph(j, p, b), 1)
                keep_pT(j, p, b, 2)
                keep_pT(j, p, b, 3)
                if more:
                    exp_trio(*next_graph(j, p, b), 2)
                if has_next and b < 3:
                    keep_qk(*nxt, (1, 3, 4)[b])
                if more:
                    exp_trio(*next_graph(j, p, b), 3)
                keep_oT_hi(j, p, b)
                if has_next and b == 2:
                    keep_qk(*nxt, 5)
                if has_after and b == 3:
                    for bb in range(QUAD):
                        keep_xT_hi(*aft, bb)

            def quad(j, p, has_next, has_after):
                for b in range(QUAD):
                    graph(j, p, b, has_next, has_after)

            for b in range(QUAD):
                keep_xT_hi(0, 0, b)
            for k in range(QK):
                keep_qk(0, 0, k)
            for b in range(QUAD):
                keep_xT_hi(0, 1, b)
            for trio in range(4):
                exp_trio(0, 0, 0, trio)
            over_quads(act, quad)

        @block.vector
        def _(dve):
            def wait_alone(semaphore, count):
                dve.compute_val(count)
                dve.wait_ge(b_loaded, 32)
                dve.wait_ge(semaphore, count)

            def keep_xT_lo(j, p, b):
                dve.wait_ge(xT_hi_done, QUAD * (2 * j + p) + b + 1)
                tok = slice(b * N, (b + 1) * N)
                nc.vector.tensor_tensor(xT_lo[:, :, tok],
                                        proj_bank[b % 2][:, 0:HIDDEN].rearrange("p (c n) -> p c n", c=CHUNKS),
                                        xT_hi[:, :, tok].bitcast(f32), ALU.subtract).then_inc(xT_lo_done, 1)

            def keep_v(j, p, b):
                dve.wait_ge(v_psum, QUAD * (2 * j + p) + b + 1)
                nc.vector.tensor_tensor(v_sb[p][:, b, :], proj_bank[V_BANK[b]][:, 0:HIDDEN], bv_sb[:, :],
                                        ALU.add).then_inc(v_done, 1)

            def bias_trio(j, p, b, trio):
                if b == 0 and trio == 0:
                    dve.wait_ge(adj_loaded[p], 16 * (j + 1))
                wait_alone(scores_psum, 4 * (QUAD * (2 * j + p) + b) + trio + 1)
                for c in range(CHUNKS):
                    u = CHUNKS * trio + c
                    last = nc.vector.tensor_tensor_reduce(
                        out=neg_a[b % 2][:, u, :], in0=score_bank[trio % 2][:, c * N:(c + 1) * N],
                        in1=adj_sb[p][:, b, :], scale=-1.0, scalar=BIG, op0=ALU.add, op1=ALU.min,
                        accum_out=neg_max[b % 2][:, u:u + 1])
                last.then_inc(neg_a_done, 1)

            def mask_sum(j, p, b, half):
                u = slice(HALF * half, HALF * (half + 1))
                dve.wait_ge(fold_done, 2 * (QUAD * (2 * j + p) + b) + half + 1)
                nc.vector.tensor_reduce(neg_sum[:, u], fold[:, u, :], AX.X, ALU.add).then_inc(mask_steps, 1)

            def mask_reciprocal(j, p, b, half):
                u = slice(HALF * half, HALF * (half + 1))
                dve.wait_ge(exp_done, 4 * (QUAD * (2 * j + p) + b) + 2 * half + 2)
                nc.vector.reciprocal(inv_sum[:, u], row_sum[b % 2][:, u]).then_inc(mask_steps, 1)

            def mask_live(j, p, b, half):
                u = slice(HALF * half, HALF * (half + 1))
                dve.wait_ge(mask_steps, MASK_STEPS * (QUAD * (2 * j + p) + b) + 3 * half + 1)
                nc.vector.tensor_tensor(live[:, u], neg_max[b % 2][:, u], neg_sum[:, u],
                                        ALU.logical_or).then_inc(mask_steps, 1)

            def mask_scale(j, p, b, half):
                u = slice(HALF * half, HALF * (half + 1))
                dve.wait_ge(mask_steps, MASK_STEPS * (QUAD * (2 * j + p) + b) + 3 * half + 3)
                nc.vector.tensor_tensor(row_scale[:, u], live[:, u], inv_sum[:, u], ALU.mult)\
                    .then_inc(scale_done, 1)

            def mask_half(j, p, b, half):
                for step in (mask_sum, mask_reciprocal, mask_live, mask_scale):
                    step(j, p, b, half)

            def keep_oT_lo(j, p, b):
                dve.wait_ge(oT_hi_done, QUAD * (2 * j + p) + b + 1)
                nc.vector.tensor_tensor(oT_lo[:, :, :],
                                        oT_bank[:, 0:HIDDEN].rearrange("p (c n) -> p c n", c=CHUNKS),
                                        oT_hi[:, :, :].bitcast(f32), ALU.subtract).then_inc(oT_lo_done, 1)

            def residual(j, p, b):
                if b == 0:
                    dve.wait_ge(xb_done, 2 * j + p + 1)
                dve.wait_ge(y_psum, QUAD * (2 * j + p) + b + 1)
                nc.vector.tensor_tensor(y_sb[:, :], y_bank[:, 0:HIDDEN], xb_sb[p][:, b, :], ALU.add)\
                    .then_inc(ln_steps, 1)

            def statistics(j, p, b):
                dve.wait_ge(ln_steps, LN_STEPS * (QUAD * (2 * j + p) + b) + 1)
                nc.vector.bn_stats(stats[:, :], y_sb[:, :]).then_inc(ln_steps, 1)

            def mean_variance(j, p, b):
                wait_alone(ln_steps, LN_STEPS * (QUAD * (2 * j + p) + b) + 2)
                nc.vector.bn_aggr(mean_var[:, :], stats[:, :]).then_inc(ln_steps, 1)

            def add_eps(j, p, b):
                dve.wait_ge(ln_steps, LN_STEPS * (QUAD * (2 * j + p) + b) + 3)
                nc.vector.tensor_scalar(var_eps[:, :], mean_var[:, 1:2], EPS, None, ALU.add)\
                    .then_inc(ln_steps, 1)

            def normalise(j, p, b):
                t = QUAD * (2 * j + p) + b
                dve.wait_ge(inv_std_done, t + 1)
                dve.wait_ge(out_stored[b], 16 * (2 * j + p) + 16)
                nc.vector.tensor_scalar(out_sb[:, b, :], y_sb[:, :], mean_var[:, 0:1], inv_std[:, 0:1],
                                        ALU.subtract, ALU.mult).then_inc(out_done, 1)

            def graph(j, p, b, has_next, has_after):
                nxt, aft = ahead(j, p, 1), ahead(j, p, 2)
                more = b + 1 < QUAD or has_next
                if more:
                    bias_trio(*next_graph(j, p, b), 0)
                    bias_trio(*next_graph(j, p, b), 1)
                if has_next and b == 3:
                    keep_v(*nxt, 2)
                if more:
                    bias_trio(*next_graph(j, p, b), 2)
                    bias_trio(*next_graph(j, p, b), 3)
                    mask_half(*next_graph(j, p, b), 0)
                if has_next and b == 3:
                    keep_v(*nxt, 3)
                keep_oT_lo(j, p, b)
                if has_next and b < 2:
                    keep_v(*nxt, b)
                if has_after and b == 3:
                    keep_xT_lo(*aft, 0)
                    keep_xT_lo(*aft, 1)
                for norm_step, mask_step in ((residual, mask_sum), (statistics, mask_reciprocal),
                                             (mean_variance, mask_live), (add_eps, mask_scale)):
                    norm_step(j, p, b)
                    if more:
                        mask_step(*next_graph(j, p, b), 1)
                normalise(j, p, b)
                if has_after and b == 3:
                    keep_xT_lo(*aft, 2)
                    keep_xT_lo(*aft, 3)

            def quad(j, p, has_next, has_after):
                for b in range(QUAD):
                    graph(j, p, b, has_next, has_after)

            for b in range(QUAD):
                keep_xT_lo(0, 0, b)
            dve.wait_ge(w_loaded, 64)
            nc.vector.tensor_scalar(w_raw[:, :, 0:HIDDEN], w_raw[:, :, 0:HIDDEN], SCALE, None,
                                    ALU.mult).then_inc(w_prep, 1)
            dve.wait_ge(w_prep, 1)
            nc.vector.tensor_copy(w_hi[:, :, :], w_raw[:, :, :]).then_inc(w_prep, 1)
            dve.wait_ge(w_prep, 2)
            nc.vector.tensor_tensor(w_lo[:, :, :], w_raw[:, :, :], w_hi[:, :, :].bitcast(f32),
                                    ALU.subtract).then_inc(w_steps, 1)
            dve.wait_ge(b_loaded, 32)
            for b in range(QUAD):
                keep_v(0, 0, b)
            for b in range(QUAD):
                keep_xT_lo(0, 1, b)
            for trio in range(4):
                bias_trio(0, 0, 0, trio)
            for half in range(2):
                mask_half(0, 0, 0, half)
            over_quads(dve, quad)

        @block.gpsimd
        def _(pool):
            def add_bo(j, p):
                pool.wait_ge(x_loaded[p], 16 * (j + 1))
                for b in range(QUAD):
                    last = nc.gpsimd.tensor_tensor(xb_sb[p][:, b, :], x_sb[p][:, b, :], bo_sb[:, :], ALU.add)
                last.then_inc(xb_done, 1)

            def fold_half(j, p, b, half):
                u = slice(HALF * half, HALF * (half + 1))
                pool.wait_ge(neg_a_done, 4 * (QUAD * (2 * j + p) + b) + 2 * half + 2)
                nc.gpsimd.tensor_tensor(fold[:, u, :], neg_a[b % 2][:, u, 0:N // 2],
                                        neg_a[b % 2][:, u, N // 2:N], ALU.add).then_inc(fold_done, 1)

            def scale_half(j, p, b, half):
                u = slice(HALF * half, HALF * (half + 1))
                pool.wait_ge(scale_done, 2 * (QUAD * (2 * j + p) + b) + half + 1)
                nc.gpsimd.tensor_tensor(probs[b % 2][:, u, :], probs[b % 2][:, u, :],
                                        row_scale[:, u].unsqueeze(2).broadcast_to([P, HALF, N]),
                                        ALU.mult).then_inc(probs_done, 1)

            def inverse_std(j, p, b):
                pool.wait_ge(ln_steps, LN_STEPS * (QUAD * (2 * j + p) + b) + 4)
                nc.gpsimd.tensor_tensor(inv_std[:, :], var_eps[:, :], minus_half[:, :], ALU.pow)\
                    .then_inc(inv_std_done, 1)

            def quad(j, p, has_next, has_after):
                for b in range(QUAD):
                    more = b + 1 < QUAD or has_next
                    if more:
                        g = next_graph(j, p, b)
                        fold_half(*g, 0)
                        fold_half(*g, 1)
                        scale_half(*g, 0)
                    inverse_std(j, p, b)
                    if more:
                        scale_half(*g, 1)
                    if has_next and b == 0:
                        add_bo(*ahead(j, p, 1))

            nc.gpsimd.memset(ident[:, :], 0.0).then_inc(ident_steps, 1)
            pool.wait_ge(ident_steps, 1)
            nc.gpsimd.affine_select(out=ident[:, :], in_=ident[:, :], compare_op=ALU.not_equal, fill=1.0,
                                    base=0, pattern=[[-1, P]], channel_multiplier=1).then_inc(ident_steps, 1)
            nc.gpsimd.memset(minus_half[:, :], -0.5).then_inc(ident_steps, 1)
            pool.wait_ge(ident_steps, 3)
            pool.wait_ge(b_loaded, 32)
            add_bo(0, 0)
            for half in range(2):
                fold_half(0, 0, 0, half)
            for half in range(2):
                scale_half(0, 0, 0, half)
            over_quads(pool, quad)


QK_BANK = (0, 1, 1, 0, 0, 1)
V_BANK = (0, 1, 0, 1)

_OUT = "out_dram"


def kernel(x, adj, L0_gnn_Wq, L0_gnn_Wk, L0_gnn_Wv, L0_gnn_bv, L0_gnn_Wo, L0_gnn_bo):
    import numpy as np
    import concourse.bacc as bacc
    from concourse.bass_utils import run_bass_kernel_spmd

    arrays = {
        "x_dram": np.ascontiguousarray(x), "adj_dram": np.ascontiguousarray(adj),
        "wq_t_dram": np.ascontiguousarray(np.asarray(L0_gnn_Wq).T),
        "wk_t_dram": np.ascontiguousarray(np.asarray(L0_gnn_Wk).T),
        "wv_t_dram": np.ascontiguousarray(np.asarray(L0_gnn_Wv).T),
        "wo_t_dram": np.ascontiguousarray(np.asarray(L0_gnn_Wo).T),
        "bv_dram": np.ascontiguousarray(L0_gnn_bv), "bo_dram": np.ascontiguousarray(L0_gnn_bo),
    }
    nc = bacc.Bacc("TRN2", target_bir_lowering=False, num_devices=1)
    args = [nc.dram_tensor(name, a.shape, mybir.dt.from_np(a.dtype), kind="ExternalInput").ap()
            for name, a in arrays.items()]
    out = nc.dram_tensor(_OUT, (BATCH, N, HIDDEN), mybir.dt.float32, kind="ExternalOutput").ap()
    attention_kernel(nc, *args, out)
    r = run_bass_kernel_spmd(nc, [arrays], core_ids=[0])
    return r.results[0][_OUT]
```

```python
import concourse.bass as bass
from concourse import mybir
from contextlib import ExitStack

BATCH, N, HIDDEN, HEADS = 128, 128, 384, 12
HEAD = HIDDEN // HEADS
P = 128
CHUNKS = HIDDEN // P
ROWS = P // HEAD
QUAD = 4
QUADS = BATCH // QUAD
TOK = QUAD * N
QK = 2 * CHUNKS
HALF = HEADS // 2
V_BANK = (0, 1, 0, 0)
X_BANK = (1, 1, 0, 1)
SCALE = float(HIDDEN) ** -0.5
EPS = 1e-5
BIG = 3.0e38
LN_STEPS = 4
MASK_STEPS = 6


def attention_kernel(nc, x, adj, wq_t, wk_t, wv_t, wo_t, bv, bo, out):
    f32 = mybir.dt.float32
    f32r = mybir.dt.float32r
    ACT = mybir.ActivationFunctionType
    ALU = mybir.AluOpType
    AX = mybir.AxisListType

    ctx = ExitStack()
    with ctx:
        def sb(name, shape, dt=f32):
            return ctx.enter_context(nc.sbuf_tensor(name, shape, dt))

        def bank(name):
            return ctx.enter_context(nc.psum_tensor(name, [P, 512], f32))

        def sem(name):
            return ctx.enter_context(nc.semaphore(name))

        x_sb = [sb(f"x_sb{p}", [P, QUAD, HIDDEN]) for p in range(2)]
        xb_sb = [sb(f"xb_sb{p}", [P, QUAD, HIDDEN]) for p in range(2)]
        adj_sb = [sb(f"adj_sb{p}", [P, QUAD, N]) for p in range(2)]
        xT_hi = sb("xT_hi", [P, CHUNKS, TOK], f32r)
        xT_lo = sb("xT_lo", [P, CHUNKS, TOK], f32r)
        qkT = [sb(f"qkT{p}", [P, QK, TOK]) for p in range(2)]
        v_sb = [sb(f"v_sb{p}", [P, QUAD, HIDDEN]) for p in range(2)]
        neg_a = [sb(f"neg_a{p}", [P, HEADS, N]) for p in range(2)]
        neg_max = [sb(f"neg_max{p}", [P, HEADS]) for p in range(2)]
        row_sum = [sb(f"row_sum{p}", [P, HEADS]) for p in range(2)]
        probs = [sb(f"probs{p}", [P, HEADS, N]) for p in range(2)]
        fold = sb("fold", [P, HEADS, N // 2])
        neg_sum = sb("neg_sum", [P, HEADS])
        live = sb("live", [P, HEADS])
        inv_sum = sb("inv_sum", [P, HEADS])
        row_scale = sb("row_scale", [P, HEADS])
        pT = sb("pT", [P, HEADS, N])
        oT_hi = sb("oT_hi", [P, CHUNKS, N], f32r)
        oT_lo = sb("oT_lo", [P, CHUNKS, N], f32r)
        y_sb = sb("y_sb", [P, HIDDEN])
        stats = sb("stats", [P, 6])
        mean_var = sb("mean_var", [P, 2])
        var_eps = sb("var_eps", [P, 1])
        minus_half = sb("minus_half", [P, 1])
        inv_std = sb("inv_std", [P, 1])
        out_sb = sb("out_sb", [P, QUAD, HIDDEN])
        w_raw = sb("w_raw", [P, CHUNKS, 4 * HIDDEN])
        w_hi = sb("w_hi", [P, CHUNKS, 4 * HIDDEN], f32r)
        w_lo = sb("w_lo", [P, CHUNKS, 4 * HIDDEN], f32r)
        bv_sb = sb("bv_sb", [P, HIDDEN])
        bo_sb = sb("bo_sb", [P, HIDDEN])
        ident = sb("ident", [P, P])

        score_bank = [bank(f"score_bank{i}") for i in range(2)]
        pT_bank = [bank(f"pT_bank{i}") for i in range(2)]
        proj_bank = [bank(f"proj_bank{i}") for i in range(2)]
        oT_bank = bank("oT_bank")
        y_bank = bank("y_bank")

        w_loaded, b_loaded = sem("w_loaded"), sem("b_loaded")
        x_loaded = [sem(f"x_loaded{p}") for p in range(2)]
        adj_loaded = [sem(f"adj_loaded{p}") for p in range(2)]
        out_stored = [sem(f"out_stored{b}") for b in range(QUAD)]
        ident_steps = sem("ident_steps")
        w_prep, w_steps = sem("w_prep"), sem("w_steps")
        xT_psum = sem("xT_psum")
        xT_hi_done = sem("xT_hi_done")
        xT_lo_done = sem("xT_lo_done")
        qk_psum = sem("qk_psum")
        qk_done = sem("qk_done")
        v_psum = sem("v_psum")
        v_done = sem("v_done")
        scores_psum = sem("scores_psum")
        neg_a_done = sem("neg_a_done")
        exp_done = sem("exp_done")
        fold_done = sem("fold_done")
        mask_steps = sem("mask_steps")
        scale_done = sem("scale_done")
        probs_done = sem("probs_done")
        pT_psum = sem("pT_psum")
        pT_done = sem("pT_done")
        oT_psum = sem("oT_psum")
        oT_hi_done = sem("oT_hi_done")
        oT_lo_done = sem("oT_lo_done")
        y_psum = sem("y_psum")
        ln_steps = sem("ln_steps")
        inv_std_done = sem("inv_std_done")
        out_done = sem("out_done")
        xb_done = sem("xb_done")

        block = ctx.enter_context(nc.Block())

        def ahead(j, p, n):
            return j + (p + n) // 2, (p + n) % 2

        def later(j, p, b, n):
            return (*ahead(j, p, (b + n) // QUAD), (b + n) % QUAD)

        def over_quads(eng, quad):
            with eng.Fori(0, QUADS // 2 - 1) as j:
                for p in range(2):
                    quad(j, p, True, True)
            for p in range(2):
                quad(QUADS // 2 - 1, p, p == 0, False)

        @block.sync
        def _(sp):
            for b in range(QUAD):
                sp.sem_inc(out_stored[b], 16)

            def load_x(graph, p):
                sp.dma_start(x_sb[p][:, :, :], x[bass.ds(graph, QUAD), :, :]
                             .rearrange("b n f -> n b f")).then_inc(x_loaded[p], 16)

            def load_adj(graph, p):
                sp.dma_start(adj_sb[p][:, :, :], adj[bass.ds(graph, QUAD), :, :]
                             .rearrange("b n m -> n b m")).then_inc(adj_loaded[p], 16)

            load_x(0, 0)
            for i, w in enumerate((wq_t, wk_t, wv_t, wo_t)):
                sp.dma_start(w_raw[:, :, i * HIDDEN:(i + 1) * HIDDEN],
                             w.rearrange("(c p) o -> p c o", p=P)).then_inc(w_loaded, 16)
            load_x(QUAD, 1)
            load_adj(0, 0)
            for vec, tile in ((bv, bv_sb), (bo, bo_sb)):
                sp.dma_start(tile[:, :], vec.rearrange("(a f) -> a f", a=1).broadcast_to([P, HIDDEN]))\
                  .then_inc(b_loaded, 16)

            def quad(j, p, has_next, has_after):
                q = 2 * j + p
                for value in (*(QUAD * q + n for n in range(2 * QUAD + 1)), 16 * q + 1):
                    sp.compute_val(value)
                if has_after:
                    sp.wait_ge(xT_psum, QUAD * q + QUAD)
                    sp.wait_ge(xb_done, QUAD * q + QUAD)
                    load_x(QUAD * q + 2 * QUAD, p)
                if has_next:
                    sp.wait_ge(neg_a_done, 16 * q + 1)
                    load_adj(QUAD * q + QUAD, 1 - p)
                for b in range(QUAD):
                    sp.wait_ge(out_done, QUAD * q + b + 1)
                    sp.dma_start(out[bass.ds(QUAD * q + b, 1), :, :].rearrange("b n f -> n (b f)"),
                                 out_sb[:, b, :]).then_inc(out_stored[b], 16)

            over_quads(sp, quad)
            for b in range(QUAD):
                sp.wait_ge(out_stored[b], 16 * (QUADS + 1))

        @block.tensor
        def _(pe):
            def split_product(dst, stat_hi, stat_lo, mov_hi, mov_lo):
                for c in range(CHUNKS):
                    nc.tensor.matmul(dst, stat_hi(c), mov_hi(c), start=(c == 0), stop=False)
                    nc.tensor.matmul(dst, stat_hi(c), mov_lo(c), start=False, stop=False)
                    last = nc.tensor.matmul(dst, stat_lo(c), mov_hi(c), start=False, stop=(c == CHUNKS - 1))
                return last

            def transpose_x(j, p, b):
                q = 2 * j + p
                if b == 0:
                    pe.wait_ge(x_loaded[p], 16 * (j + 1))
                if b == 1 or b == 3:
                    pe.wait_ge(xT_lo_done, QUAD * q + (b + 1) // 2)
                elif not (isinstance(q, int) and q == 0):
                    pe.wait_ge(v_done, QUAD * q - 2 + b)
                for c in range(CHUNKS):
                    last = nc.tensor.transpose(proj_bank[X_BANK[b]][:, c * P:(c + 1) * P],
                                               x_sb[p][:, b, c * P:(c + 1) * P], ident[:, :])
                last.then_inc(xT_psum, 1)

            def project_qk(j, p, k):
                q = 2 * j + p
                if k == 0:
                    pe.wait_ge(xT_lo_done, QUAD * q + QUAD)
                if k >= 2:
                    pe.wait_ge(qk_done, QK * q + k - 1)
                split_product(proj_bank[k % 2][:, :],
                              lambda c: w_hi[:, c, k * P:(k + 1) * P], lambda c: w_lo[:, c, k * P:(k + 1) * P],
                              lambda c: xT_hi[:, c, :], lambda c: xT_lo[:, c, :]).then_inc(qk_psum, 1)

            def project_v(j, p, b):
                q = 2 * j + p
                if b < 2:
                    pe.wait_ge(qk_done, QK * q + QK - 1 + b)
                else:
                    pe.wait_ge(v_done, QUAD * q + (1, 3)[b - 2])
                tok = slice(b * N, (b + 1) * N)
                split_product(proj_bank[V_BANK[b]][:, 0:HIDDEN],
                              lambda c: xT_hi[:, c, tok], lambda c: xT_lo[:, c, tok],
                              lambda c: w_hi[:, c, 2 * HIDDEN:3 * HIDDEN],
                              lambda c: w_lo[:, c, 2 * HIDDEN:3 * HIDDEN]).then_inc(v_psum, 1)

            def scores(j, p, b, pair):
                t = QUAD * (2 * j + p) + b
                if b == 0 and pair == 0:
                    pe.wait_ge(qk_done, QK * (2 * j + p) + QK)
                if pair == 1 or not (isinstance(t, int) and t == 0):
                    pe.wait_ge(neg_a_done, 4 * t + 2 * pair)
                tok = slice(b * N, (b + 1) * N)
                for c in range(CHUNKS):
                    for r in range(2):
                        row = slice(HEAD * (2 * pair + r), HEAD * (2 * pair + r + 1))
                        last = nc.tensor.matmul(score_bank[r][:, c * N:(c + 1) * N], qkT[p][row, c, tok],
                                                qkT[p][row, CHUNKS + c, tok], start=True, stop=True)
                        if c == CHUNKS - 1:
                            last.then_inc(scores_psum, 1)

            def transpose_probs(j, p, b, pair):
                t = QUAD * (2 * j + p) + b
                pe.wait_ge(probs_done, 2 * t + pair + 1)
                for r in range(2):
                    trio = 2 * pair + r
                    if pair == 1:
                        pe.wait_ge(pT_done, 4 * t + r + 1)
                    for c in range(CHUNKS):
                        last = nc.tensor.transpose(pT_bank[r][:, c * N:(c + 1) * N],
                                                   probs[b % 2][:, 3 * trio + c, :], ident[:, :])
                    last.then_inc(pT_psum, 1)

            def attend(j, p, b):
                t = QUAD * (2 * j + p) + b
                if b == 0:
                    pe.wait_ge(v_done, t + QUAD)
                pe.wait_ge(pT_done, 4 * t + 4)
                for c in range(CHUNKS):
                    for r in range(ROWS):
                        h = ROWS * c + r
                        last = nc.tensor.matmul(oT_bank[HEAD * r:HEAD * (r + 1), c * N:(c + 1) * N],
                                                v_sb[p][:, b, HEAD * h:HEAD * (h + 1)],
                                                pT[:, CHUNKS * r + c, :], start=True, stop=True)
                last.then_inc(oT_psum, 1)

            def project_out(j, p, b):
                t = QUAD * (2 * j + p) + b
                pe.wait_ge(oT_lo_done, t + 1)
                split_product(y_bank[:, 0:HIDDEN],
                              lambda c: oT_hi[:, c, :], lambda c: oT_lo[:, c, :],
                              lambda c: w_hi[:, c, 3 * HIDDEN:4 * HIDDEN],
                              lambda c: w_lo[:, c, 3 * HIDDEN:4 * HIDDEN]).then_inc(y_psum, 1)

            def graph(j, p, b, has_next, has_after):
                nxt, aft = ahead(j, p, 1), ahead(j, p, 2)

                def cover(step):
                    if has_next and b < 2:
                        project_qk(*nxt, 3 * b + step)
                    elif has_next and b == 2:
                        project_v(*nxt, step)

                cover(0)
                if has_after and b == 3:
                    transpose_x(*aft, 0)
                transpose_probs(j, p, b, 0)
                if b + 1 < QUAD or has_next:
                    scores(*later(j, p, b, 1), 1)
                transpose_probs(j, p, b, 1)
                cover(1)
                if has_next and b == 3:
                    project_v(*nxt, 3)
                attend(j, p, b)
                if has_after and b == 3:
                    transpose_x(*aft, 1)
                if b + 2 < QUAD or has_next:
                    scores(*later(j, p, b, 2), 0)
                cover(2)
                if has_after and b == 3:
                    transpose_x(*aft, 2)
                    transpose_x(*aft, 3)
                project_out(j, p, b)

            def quad(j, p, has_next, has_after):
                for b in range(QUAD):
                    graph(j, p, b, has_next, has_after)

            pe.wait_ge(ident_steps, 2)
            for b in range(QUAD):
                transpose_x(0, 0, b)
            pe.wait_ge(w_steps, 1)
            for k in range(QK):
                project_qk(0, 0, k)
            for b in range(QUAD - 1):
                project_v(0, 0, b)
            transpose_x(0, 1, 0)
            project_v(0, 0, 3)
            for b in range(1, QUAD):
                transpose_x(0, 1, b)
            scores(0, 0, 0, 0)
            scores(0, 0, 0, 1)
            scores(0, 0, 1, 0)
            over_quads(pe, quad)

        @block.scalar
        def _(act):
            def keep_xT_hi(j, p, b):
                act.wait_ge(xT_psum, QUAD * (2 * j + p) + b + 1)
                nc.scalar.activation(xT_hi[:, :, b * N:(b + 1) * N],
                                     proj_bank[X_BANK[b]][:, 0:HIDDEN].rearrange("p (c n) -> p c n", c=CHUNKS),
                                     ACT.Copy).then_inc(xT_hi_done, 1)

            def keep_qk(j, p, k):
                act.wait_ge(qk_psum, QK * (2 * j + p) + k + 1)
                nc.scalar.activation(qkT[p][:, k, :], proj_bank[k % 2][:, :], ACT.Copy)\
                    .then_inc(qk_done, 1)

            def exp_trio(j, p, b, trio):
                act.wait_ge(neg_a_done, 4 * (QUAD * (2 * j + p) + b) + trio + 1)
                for u in range(CHUNKS * trio, CHUNKS * (trio + 1)):
                    last = nc.scalar.activation(probs[b % 2][:, u, :], neg_a[b % 2][:, u, :], ACT.Exp,
                                                bias=neg_max[b % 2][:, u:u + 1], scale=-1.0,
                                                accum_out=row_sum[b % 2][:, u:u + 1])
                last.then_inc(exp_done, 1)

            def keep_pT(j, p, b, trio):
                act.wait_ge(pT_psum, 4 * (QUAD * (2 * j + p) + b) + trio + 1)
                nc.scalar.activation(pT[:, CHUNKS * trio:CHUNKS * (trio + 1), :],
                                     pT_bank[trio % 2][:, 0:HIDDEN].rearrange("p (c n) -> p c n", c=CHUNKS),
                                     ACT.Copy).then_inc(pT_done, 1)

            def keep_oT_hi(j, p, b):
                act.wait_ge(oT_psum, QUAD * (2 * j + p) + b + 1)
                nc.scalar.activation(oT_hi[:, :, :],
                                     oT_bank[:, 0:HIDDEN].rearrange("p (c n) -> p c n", c=CHUNKS),
                                     ACT.Copy).then_inc(oT_hi_done, 1)

            def graph(j, p, b, has_next, has_after):
                nxt, aft = ahead(j, p, 1), ahead(j, p, 2)
                if has_next and b < 2:
                    keep_qk(*nxt, 3 * b)
                if has_after and b == 3:
                    keep_xT_hi(*aft, 0)
                for trio in range(4):
                    keep_pT(j, p, b, trio)
                if b + 1 < QUAD or has_next:
                    exp_trio(*later(j, p, b, 1), 2)
                if has_next and b < 2:
                    keep_qk(*nxt, 3 * b + 1)
                keep_oT_hi(j, p, b)
                if has_after and b == 3:
                    keep_xT_hi(*aft, 1)
                if b + 1 < QUAD or has_next:
                    exp_trio(*later(j, p, b, 1), 3)
                if has_after and b == 3:
                    keep_xT_hi(*aft, 2)
                    keep_xT_hi(*aft, 3)
                if b + 2 < QUAD or has_next:
                    exp_trio(*later(j, p, b, 2), 0)
                if has_next and b < 2:
                    keep_qk(*nxt, 3 * b + 2)
                if b + 2 < QUAD or has_next:
                    exp_trio(*later(j, p, b, 2), 1)

            def quad(j, p, has_next, has_after):
                for b in range(QUAD):
                    graph(j, p, b, has_next, has_after)

            for b in range(QUAD):
                keep_xT_hi(0, 0, b)
            for k in range(QK):
                keep_qk(0, 0, k)
            for b in range(QUAD):
                keep_xT_hi(0, 1, b)
            for trio in range(4):
                exp_trio(0, 0, 0, trio)
            for trio in range(2):
                exp_trio(0, 0, 1, trio)
            over_quads(act, quad)

        @block.vector
        def _(dve):
            def wait_alone(semaphore, count):
                dve.compute_val(count)
                dve.wait_ge(b_loaded, 32)
                dve.wait_ge(semaphore, count)

            def keep_xT_lo(j, p, b):
                dve.wait_ge(xT_hi_done, QUAD * (2 * j + p) + b + 1)
                tok = slice(b * N, (b + 1) * N)
                nc.vector.tensor_tensor(xT_lo[:, :, tok],
                                        proj_bank[X_BANK[b]][:, 0:HIDDEN].rearrange("p (c n) -> p c n", c=CHUNKS),
                                        xT_hi[:, :, tok].bitcast(f32), ALU.subtract).then_inc(xT_lo_done, 1)

            def keep_v(j, p, b):
                dve.wait_ge(v_psum, QUAD * (2 * j + p) + b + 1)
                nc.vector.tensor_tensor(v_sb[p][:, b, :], proj_bank[V_BANK[b]][:, 0:HIDDEN], bv_sb[:, :],
                                        ALU.add).then_inc(v_done, 1)

            def bias_trio(j, p, b, trio):
                if b == 0 and trio == 0:
                    dve.wait_ge(adj_loaded[p], 16 * (j + 1))
                wait_alone(scores_psum, 4 * (QUAD * (2 * j + p) + b) + trio + 1)
                for c in range(CHUNKS):
                    u = CHUNKS * trio + c
                    last = nc.vector.tensor_tensor_reduce(
                        out=neg_a[b % 2][:, u, :], in0=score_bank[trio % 2][:, c * N:(c + 1) * N],
                        in1=adj_sb[p][:, b, :], scale=-1.0, scalar=BIG, op0=ALU.add, op1=ALU.min,
                        accum_out=neg_max[b % 2][:, u:u + 1])
                last.then_inc(neg_a_done, 1)

            def mask_sum(j, p, b, half):
                u = slice(HALF * half, HALF * (half + 1))
                dve.wait_ge(fold_done, 2 * (QUAD * (2 * j + p) + b) + half + 1)
                nc.vector.tensor_reduce(neg_sum[:, u], fold[:, u, :], AX.X, ALU.add).then_inc(mask_steps, 1)

            def mask_reciprocal(j, p, b, half):
                u = slice(HALF * half, HALF * (half + 1))
                dve.wait_ge(exp_done, 4 * (QUAD * (2 * j + p) + b) + 2 * half + 2)
                nc.vector.reciprocal(inv_sum[:, u], row_sum[b % 2][:, u]).then_inc(mask_steps, 1)

            def mask_live(j, p, b, half):
                u = slice(HALF * half, HALF * (half + 1))
                dve.wait_ge(mask_steps, MASK_STEPS * (QUAD * (2 * j + p) + b) + 3 * half + 1)
                nc.vector.tensor_tensor(live[:, u], neg_max[b % 2][:, u], neg_sum[:, u],
                                        ALU.logical_or).then_inc(mask_steps, 1)

            def mask_scale(j, p, b, half):
                u = slice(HALF * half, HALF * (half + 1))
                dve.wait_ge(mask_steps, MASK_STEPS * (QUAD * (2 * j + p) + b) + 3 * half + 3)
                nc.vector.tensor_tensor(row_scale[:, u], live[:, u], inv_sum[:, u], ALU.mult)\
                    .then_inc(scale_done, 1)

            def mask_half(j, p, b, half):
                for step in (mask_sum, mask_reciprocal, mask_live, mask_scale):
                    step(j, p, b, half)

            def keep_oT_lo(j, p, b):
                dve.wait_ge(oT_hi_done, QUAD * (2 * j + p) + b + 1)
                nc.vector.tensor_tensor(oT_lo[:, :, :],
                                        oT_bank[:, 0:HIDDEN].rearrange("p (c n) -> p c n", c=CHUNKS),
                                        oT_hi[:, :, :].bitcast(f32), ALU.subtract).then_inc(oT_lo_done, 1)

            def residual(j, p, b):
                dve.wait_ge(xb_done, QUAD * (2 * j + p) + b + 1)
                dve.wait_ge(y_psum, QUAD * (2 * j + p) + b + 1)
                nc.vector.tensor_tensor(y_sb[:, :], y_bank[:, 0:HIDDEN], xb_sb[p][:, b, :], ALU.add)\
                    .then_inc(ln_steps, 1)

            def statistics(j, p, b):
                dve.wait_ge(ln_steps, LN_STEPS * (QUAD * (2 * j + p) + b) + 1)
                nc.vector.bn_stats(stats[:, :], y_sb[:, :]).then_inc(ln_steps, 1)

            def mean_variance(j, p, b):
                wait_alone(ln_steps, LN_STEPS * (QUAD * (2 * j + p) + b) + 2)
                nc.vector.bn_aggr(mean_var[:, :], stats[:, :]).then_inc(ln_steps, 1)

            def add_eps(j, p, b):
                dve.wait_ge(ln_steps, LN_STEPS * (QUAD * (2 * j + p) + b) + 3)
                nc.vector.tensor_scalar(var_eps[:, :], mean_var[:, 1:2], EPS, None, ALU.add)\
                    .then_inc(ln_steps, 1)

            def normalise(j, p, b):
                t = QUAD * (2 * j + p) + b
                dve.wait_ge(inv_std_done, t + 1)
                dve.wait_ge(out_stored[b], 16 * (2 * j + p) + 16)
                nc.vector.tensor_scalar(out_sb[:, b, :], y_sb[:, :], mean_var[:, 0:1], inv_std[:, 0:1],
                                        ALU.subtract, ALU.mult).then_inc(out_done, 1)

            def graph(j, p, b, has_next, has_after):
                nxt, aft = ahead(j, p, 1), ahead(j, p, 2)
                more = b + 1 < QUAD or has_next
                more2 = b + 2 < QUAD or has_next
                if has_next and b == 2:
                    keep_v(*nxt, 0)
                if has_after and b == 3:
                    keep_xT_lo(*aft, 0)
                if more:
                    bias_trio(*later(j, p, b, 1), 2)
                    bias_trio(*later(j, p, b, 1), 3)
                if has_next and b >= 2:
                    keep_v(*nxt, (1, 3)[b - 2])
                keep_oT_lo(j, p, b)
                if has_after and b == 3:
                    keep_xT_lo(*aft, 1)
                if more2:
                    bias_trio(*later(j, p, b, 2), 0)
                if has_after and b == 3:
                    keep_xT_lo(*aft, 2)
                    keep_xT_lo(*aft, 3)
                if more2:
                    bias_trio(*later(j, p, b, 2), 1)
                if more:
                    mask_half(*later(j, p, b, 1), 1)
                if has_next and b == 2:
                    keep_v(*nxt, 2)
                for norm_step, mask_step in ((residual, mask_sum), (statistics, mask_reciprocal),
                                             (mean_variance, mask_live), (add_eps, mask_scale)):
                    norm_step(j, p, b)
                    if more2:
                        mask_step(*later(j, p, b, 2), 0)
                normalise(j, p, b)

            def quad(j, p, has_next, has_after):
                for b in range(QUAD):
                    graph(j, p, b, has_next, has_after)

            for b in range(QUAD):
                keep_xT_lo(0, 0, b)
            dve.wait_ge(w_loaded, 64)
            nc.vector.tensor_scalar(w_raw[:, :, 0:HIDDEN], w_raw[:, :, 0:HIDDEN], SCALE, None,
                                    ALU.mult).then_inc(w_prep, 1)
            dve.wait_ge(w_prep, 1)
            nc.vector.tensor_copy(w_hi[:, :, :], w_raw[:, :, :]).then_inc(w_prep, 1)
            dve.wait_ge(w_prep, 2)
            nc.vector.tensor_tensor(w_lo[:, :, :], w_raw[:, :, :], w_hi[:, :, :].bitcast(f32),
                                    ALU.subtract).then_inc(w_steps, 1)
            dve.wait_ge(b_loaded, 32)
            for b in range(QUAD - 1):
                keep_v(0, 0, b)
            keep_xT_lo(0, 1, 0)
            keep_v(0, 0, 3)
            for b in range(1, QUAD):
                keep_xT_lo(0, 1, b)
            for trio in range(4):
                bias_trio(0, 0, 0, trio)
            for half in range(2):
                mask_half(0, 0, 0, half)
            for trio in range(2):
                bias_trio(0, 0, 1, trio)
            mask_half(0, 0, 1, 0)
            over_quads(dve, quad)

        @block.gpsimd
        def _(pool):
            def add_bo(j, p, b):
                if b == 0:
                    pool.wait_ge(x_loaded[p], 16 * (j + 1))
                nc.gpsimd.tensor_tensor(xb_sb[p][:, b, :], x_sb[p][:, b, :], bo_sb[:, :], ALU.add)\
                    .then_inc(xb_done, 1)

            def fold_half(j, p, b, half):
                u = slice(HALF * half, HALF * (half + 1))
                pool.wait_ge(neg_a_done, 4 * (QUAD * (2 * j + p) + b) + 2 * half + 2)
                nc.gpsimd.tensor_tensor(fold[:, u, :], neg_a[b % 2][:, u, 0:N // 2],
                                        neg_a[b % 2][:, u, N // 2:N], ALU.add).then_inc(fold_done, 1)

            def scale_half(j, p, b, half):
                u = slice(HALF * half, HALF * (half + 1))
                pool.wait_ge(scale_done, 2 * (QUAD * (2 * j + p) + b) + half + 1)
                nc.gpsimd.tensor_tensor(probs[b % 2][:, u, :], probs[b % 2][:, u, :],
                                        row_scale[:, u].unsqueeze(2).broadcast_to([P, HALF, N]),
                                        ALU.mult).then_inc(probs_done, 1)

            def inverse_std(j, p, b):
                pool.wait_ge(ln_steps, LN_STEPS * (QUAD * (2 * j + p) + b) + 4)
                nc.gpsimd.tensor_tensor(inv_std[:, :], var_eps[:, :], minus_half[:, :], ALU.pow)\
                    .then_inc(inv_std_done, 1)

            def quad(j, p, has_next, has_after):
                for b in range(QUAD):
                    more = b + 1 < QUAD or has_next
                    if more:
                        scale_half(*later(j, p, b, 1), 0)
                        fold_half(*later(j, p, b, 1), 1)
                    if has_next:
                        add_bo(*ahead(j, p, 1), b)
                    if more:
                        scale_half(*later(j, p, b, 1), 1)
                    if b + 2 < QUAD or has_next:
                        fold_half(*later(j, p, b, 2), 0)
                    inverse_std(j, p, b)

            nc.gpsimd.memset(ident[:, :], 0.0).then_inc(ident_steps, 1)
            pool.wait_ge(ident_steps, 1)
            nc.gpsimd.affine_select(out=ident[:, :], in_=ident[:, :], compare_op=ALU.not_equal, fill=1.0,
                                    base=0, pattern=[[-1, P]], channel_multiplier=1).then_inc(ident_steps, 1)
            nc.gpsimd.memset(minus_half[:, :], -0.5).then_inc(ident_steps, 1)
            pool.wait_ge(ident_steps, 3)
            pool.wait_ge(b_loaded, 32)
            for b in range(QUAD):
                add_bo(0, 0, b)
            for half in range(2):
                fold_half(0, 0, 0, half)
            for half in range(2):
                scale_half(0, 0, 0, half)
            fold_half(0, 0, 1, 0)
            over_quads(pool, quad)


_OUT = "out_dram"


def kernel(x, adj, L0_gnn_Wq, L0_gnn_Wk, L0_gnn_Wv, L0_gnn_bv, L0_gnn_Wo, L0_gnn_bo):
    import numpy as np
    import concourse.bacc as bacc
    from concourse.bass_utils import run_bass_kernel_spmd

    arrays = {
        "x_dram": np.ascontiguousarray(x), "adj_dram": np.ascontiguousarray(adj),
        "wq_t_dram": np.ascontiguousarray(np.asarray(L0_gnn_Wq).T),
        "wk_t_dram": np.ascontiguousarray(np.asarray(L0_gnn_Wk).T),
        "wv_t_dram": np.ascontiguousarray(np.asarray(L0_gnn_Wv).T),
        "wo_t_dram": np.ascontiguousarray(np.asarray(L0_gnn_Wo).T),
        "bv_dram": np.ascontiguousarray(L0_gnn_bv), "bo_dram": np.ascontiguousarray(L0_gnn_bo),
    }
    nc = bacc.Bacc("TRN2", target_bir_lowering=False, num_devices=1)
    args = [nc.dram_tensor(name, a.shape, mybir.dt.from_np(a.dtype), kind="ExternalInput").ap()
            for name, a in arrays.items()]
    out = nc.dram_tensor(_OUT, (BATCH, N, HIDDEN), mybir.dt.float32, kind="ExternalOutput").ap()
    attention_kernel(nc, *args, out)
    r = run_bass_kernel_spmd(nc, [arrays], core_ids=[0])
    return r.results[0][_OUT]
```

```python
import concourse.bass as bass
from concourse import mybir
from contextlib import ExitStack

BATCH, N, HIDDEN, HEADS = 128, 128, 384, 12
HEAD = HIDDEN // HEADS
P = 128
CHUNKS = HIDDEN // P
ROWS = P // HEAD
QUAD = 4
QUADS = BATCH // QUAD
TOK = QUAD * N
QK = 2 * CHUNKS
HALF = HEADS // 2
SCALE = float(HIDDEN) ** -0.5
EPS = 1e-5
WARM_UP = 30
BIG = 3.0e38
LN_STEPS = 4
W_PARTS = ([(slice(k * P, (k + 1) * P), SCALE) for k in range(CHUNKS)] +
           [(slice(i * HIDDEN, (i + 1) * HIDDEN), 1.0) for i in range(1, 4)])
MASK_STEPS = 6


def attention_kernel(nc, x, xT, adj, wq_t, wk_t, wv_t, wo_t, bv, bo, out):
    f32 = mybir.dt.float32
    f32r = mybir.dt.float32r
    ACT = mybir.ActivationFunctionType
    ALU = mybir.AluOpType
    AX = mybir.AxisListType

    ctx = ExitStack()
    with ctx:
        def sb(name, shape, dt=f32):
            return ctx.enter_context(nc.sbuf_tensor(name, shape, dt))

        def bank(name):
            return ctx.enter_context(nc.psum_tensor(name, [P, 512], f32))

        def sem(name):
            return ctx.enter_context(nc.semaphore(name))

        x_sb = [sb(f"x_sb{p}", [P, QUAD, HIDDEN]) for p in range(2)]
        adj_sb = [sb(f"adj_sb{p}", [P, QUAD, N]) for p in range(2)]
        xT_raw = sb("xT_raw", [P, CHUNKS, TOK])
        xT_hi = [sb(f"xT_hi{p}", [P, CHUNKS, TOK], f32r) for p in range(2)]
        xT_lo = [sb(f"xT_lo{p}", [P, CHUNKS, TOK], f32r) for p in range(2)]
        qkT = [sb(f"qkT{p}", [P, QK, TOK]) for p in range(2)]
        v_sb = [sb(f"v_sb{p}", [P, QUAD, HIDDEN]) for p in range(2)]
        neg_a = [sb(f"neg_a{p}", [P, HEADS, N]) for p in range(2)]
        neg_max = [sb(f"neg_max{p}", [P, HEADS]) for p in range(2)]
        row_sum = [sb(f"row_sum{p}", [P, HEADS]) for p in range(2)]
        probs = [sb(f"probs{p}", [P, HEADS, N]) for p in range(2)]
        fold = sb("fold", [P, HEADS, N // 2])
        neg_sum = sb("neg_sum", [P, HEADS])
        live = sb("live", [P, HEADS])
        inv_sum = sb("inv_sum", [P, HEADS])
        row_scale = sb("row_scale", [P, HEADS])
        pT = sb("pT", [P, HEADS, N])
        oT_hi = sb("oT_hi", [P, CHUNKS, N], f32r)
        oT_lo = sb("oT_lo", [P, CHUNKS, N], f32r)
        y_sb = sb("y_sb", [P, HIDDEN])
        stats = sb("stats", [P, 6])
        mean_var = sb("mean_var", [P, 2])
        var_eps = sb("var_eps", [P, 1])
        minus_half = sb("minus_half", [P, 1])
        inv_std = sb("inv_std", [P, 1])
        out_sb = sb("out_sb", [P, QUAD, HIDDEN])
        w_raw = sb("w_raw", [P, CHUNKS, 4 * HIDDEN])
        w_hi = sb("w_hi", [P, CHUNKS, 4 * HIDDEN], f32r)
        w_lo = sb("w_lo", [P, CHUNKS, 4 * HIDDEN], f32r)
        bv_sb = sb("bv_sb", [P, HIDDEN])
        bo_sb = sb("bo_sb", [P, HIDDEN])
        ident = sb("ident", [P, P])

        score_bank = [bank(f"score_bank{i}") for i in range(2)]
        pT_bank = [bank(f"pT_bank{i}") for i in range(2)]
        proj_bank = [bank(f"proj_bank{i}") for i in range(2)]
        oT_bank = bank("oT_bank")
        y_bank = bank("y_bank")

        w_loaded = [sem(f"w_loaded_{name}") for name in "qkvo"]
        b_loaded = sem("b_loaded")
        xT_loaded = sem("xT_loaded")
        x_loaded = [sem(f"x_loaded{p}") for p in range(2)]
        adj_loaded = [sem(f"adj_loaded{p}") for p in range(2)]
        out_stored = [sem(f"out_stored{b}") for b in range(QUAD)]
        ident_steps = sem("ident_steps")
        w_hi_done = sem("w_hi_done")
        w_lo_done = sem("w_lo_done")
        xT_hi_done = sem("xT_hi_done")
        xT_lo_done = sem("xT_lo_done")
        qk_psum = sem("qk_psum")
        qk_done = sem("qk_done")
        v_psum = sem("v_psum")
        v_done = sem("v_done")
        scores_psum = sem("scores_psum")
        neg_a_done = sem("neg_a_done")
        exp_done = sem("exp_done")
        fold_done = sem("fold_done")
        mask_steps = sem("mask_steps")
        scale_done = sem("scale_done")
        probs_done = sem("probs_done")
        pT_psum = sem("pT_psum")
        pT_done = sem("pT_done")
        oT_psum = sem("oT_psum")
        oT_hi_done = sem("oT_hi_done")
        oT_lo_done = sem("oT_lo_done")
        y_psum = sem("y_psum")
        ln_steps = sem("ln_steps")
        inv_std_done = sem("inv_std_done")
        out_done = sem("out_done")
        xb_done = sem("xb_done")

        block = ctx.enter_context(nc.Block())

        def ahead(j, p, n):
            return j + (p + n) // 2, (p + n) % 2

        def later(j, p, b, n):
            return (*ahead(j, p, (b + n) // QUAD), (b + n) % QUAD)

        def over_quads(eng, quad):
            with eng.Fori(0, QUADS // 2 - 1) as j:
                for p in range(2):
                    quad(j, p, True, True)
            for p in range(2):
                quad(QUADS // 2 - 1, p, p == 0, False)

        @block.sync
        def _(sp):
            for b in range(QUAD):
                sp.sem_inc(out_stored[b], 16)

            def load_x(graph, p):
                sp.dma_start(x_sb[p][:, :, :], x[bass.ds(graph, QUAD), :, :]
                             .rearrange("b n f -> n b f")).then_inc(x_loaded[p], 16)

            def load_adj(graph, p):
                sp.dma_start(adj_sb[p][:, :, :], adj[bass.ds(graph, QUAD), :, :]
                             .rearrange("b n m -> n b m")).then_inc(adj_loaded[p], 16)

            def load_xT(quad):
                sp.dma_start(xT_raw[:, :, :], xT[bass.ds(quad, 1), :, :, :]
                             .rearrange("q p c t -> p (q c) t")).then_inc(xT_loaded, 16)

            load_xT(0)
            for i, w in enumerate((wq_t, wk_t, wv_t, wo_t)):
                sp.dma_start(w_raw[:, :, i * HIDDEN:(i + 1) * HIDDEN],
                             w.rearrange("(c p) o -> p c o", p=P)).then_inc(w_loaded[i], 16)
            for vec, tile in ((bv, bv_sb), (bo, bo_sb)):
                sp.dma_start(tile[:, :], vec.rearrange("(a f) -> a f", a=1).broadcast_to([P, HIDDEN]))\
                  .then_inc(b_loaded, 16)
            load_adj(0, 0)
            sp.wait_ge(xT_lo_done, CHUNKS)
            load_xT(1)
            load_x(0, 0)
            load_x(QUAD, 1)

            def quad(j, p, has_next, has_after):
                q = 2 * j + p
                for value in (*(QUAD * q + n for n in range(2 * QUAD + 1)), 16 * q + 1,
                              CHUNKS * q + 2 * CHUNKS, q + 2):
                    sp.compute_val(value)
                if has_next:
                    sp.wait_ge(neg_a_done, 16 * q + 1)
                    load_adj(QUAD * q + QUAD, 1 - p)
                if has_after:
                    sp.wait_ge(xT_lo_done, CHUNKS * q + 2 * CHUNKS)
                    load_xT(q + 2)
                for b in range(QUAD):
                    sp.wait_ge(out_done, QUAD * q + b + 1)
                    sp.dma_start(out[bass.ds(QUAD * q + b, 1), :, :].rearrange("b n f -> n (b f)"),
                                 out_sb[:, b, :]).then_inc(out_stored[b], 16)
                if has_after:
                    load_x(QUAD * q + 2 * QUAD, p)

            over_quads(sp, quad)
            for b in range(QUAD):
                sp.wait_ge(out_stored[b], 16 * (QUADS + 1))

        @block.tensor
        def _(pe):
            def split_product(dst, stat_hi, stat_lo, mov_hi, mov_lo):
                for c in range(CHUNKS):
                    nc.tensor.matmul(dst, stat_hi(c), mov_hi(c), start=(c == 0), stop=False)
                    nc.tensor.matmul(dst, stat_hi(c), mov_lo(c), start=False, stop=False)
                    last = nc.tensor.matmul(dst, stat_lo(c), mov_hi(c), start=False, stop=(c == CHUNKS - 1))
                return last

            def project_qk(j, p, k):
                q = 2 * j + p
                first = isinstance(q, int) and q == 0
                if k == 0:
                    pe.wait_ge(xT_lo_done, CHUNKS * q + CHUNKS)
                if k >= 2:
                    pe.wait_ge(qk_done, QK * q + k - 1)
                elif not first:
                    pe.wait_ge(v_done, QUAD * q - 1 + k)
                split_product(proj_bank[k % 2][:, :],
                              lambda c: w_hi[:, c, k * P:(k + 1) * P], lambda c: w_lo[:, c, k * P:(k + 1) * P],
                              lambda c: xT_hi[p][:, c, :], lambda c: xT_lo[p][:, c, :]).then_inc(qk_psum, 1)

            def project_v(j, p, b):
                q = 2 * j + p
                if b < 2:
                    pe.wait_ge(qk_done, QK * q + QK - 1 + b)
                else:
                    pe.wait_ge(v_done, QUAD * q + b - 1)
                tok = slice(b * N, (b + 1) * N)
                split_product(proj_bank[b % 2][:, 0:HIDDEN],
                              lambda c: xT_hi[p][:, c, tok], lambda c: xT_lo[p][:, c, tok],
                              lambda c: w_hi[:, c, 2 * HIDDEN:3 * HIDDEN],
                              lambda c: w_lo[:, c, 2 * HIDDEN:3 * HIDDEN]).then_inc(v_psum, 1)

            def scores(j, p, b, pair):
                t = QUAD * (2 * j + p) + b
                if b == 0 and pair == 0:
                    pe.wait_ge(qk_done, QK * (2 * j + p) + QK)
                if pair == 1 or not (isinstance(t, int) and t == 0):
                    pe.wait_ge(neg_a_done, 4 * t + 2 * pair)
                tok = slice(b * N, (b + 1) * N)
                for c in range(CHUNKS):
                    for r in range(2):
                        row = slice(HEAD * (2 * pair + r), HEAD * (2 * pair + r + 1))
                        last = nc.tensor.matmul(score_bank[r][:, c * N:(c + 1) * N], qkT[p][row, c, tok],
                                                qkT[p][row, CHUNKS + c, tok], start=True, stop=True)
                        if c == CHUNKS - 1:
                            last.then_inc(scores_psum, 1)

            def transpose_probs(j, p, b, pair):
                t = QUAD * (2 * j + p) + b
                pe.wait_ge(probs_done, 2 * t + pair + 1)
                for r in range(2):
                    trio = 2 * pair + r
                    if pair == 1:
                        pe.wait_ge(pT_done, 4 * t + r + 1)
                    for c in range(CHUNKS):
                        last = nc.tensor.transpose(pT_bank[r][:, c * N:(c + 1) * N],
                                                   probs[b % 2][:, 3 * trio + c, :], ident[:, :])
                    last.then_inc(pT_psum, 1)

            def attend(j, p, b):
                t = QUAD * (2 * j + p) + b
                if b == 0:
                    pe.wait_ge(v_done, t + QUAD)
                pe.wait_ge(pT_done, 4 * t + 4)
                for c in range(CHUNKS):
                    for r in range(ROWS):
                        h = ROWS * c + r
                        last = nc.tensor.matmul(oT_bank[HEAD * r:HEAD * (r + 1), c * N:(c + 1) * N],
                                                v_sb[p][:, b, HEAD * h:HEAD * (h + 1)],
                                                pT[:, CHUNKS * r + c, :], start=True, stop=True)
                last.then_inc(oT_psum, 1)

            def project_out(j, p, b):
                t = QUAD * (2 * j + p) + b
                pe.wait_ge(oT_lo_done, t + 1)
                split_product(y_bank[:, 0:HIDDEN],
                              lambda c: oT_hi[:, c, :], lambda c: oT_lo[:, c, :],
                              lambda c: w_hi[:, c, 3 * HIDDEN:4 * HIDDEN],
                              lambda c: w_lo[:, c, 3 * HIDDEN:4 * HIDDEN]).then_inc(y_psum, 1)

            def graph(j, p, b, has_next, has_after):
                nxt = ahead(j, p, 1)

                def cover(step):
                    if has_next and b < 2:
                        project_qk(*nxt, 3 * b + step)
                    elif has_next and step > 0:
                        project_v(*nxt, 2 * (b - 2) + step - 1)

                cover(0)
                transpose_probs(j, p, b, 0)
                if b + 1 < QUAD or has_next:
                    scores(*later(j, p, b, 1), 1)
                transpose_probs(j, p, b, 1)
                cover(1)
                attend(j, p, b)
                if b + 2 < QUAD or has_next:
                    scores(*later(j, p, b, 2), 0)
                cover(2)
                project_out(j, p, b)

            def quad(j, p, has_next, has_after):
                for b in range(QUAD):
                    graph(j, p, b, has_next, has_after)

            pe.wait_ge(ident_steps, 2)
            for _ in range(WARM_UP):
                nc.tensor.transpose(y_bank[:, 0:P], ident[:, :], ident[:, :])
            for k in range(QK):
                if k <= CHUNKS:
                    pe.wait_ge(w_lo_done, k + 1)
                project_qk(0, 0, k)
            pe.wait_ge(w_lo_done, len(W_PARTS))
            scores(0, 0, 0, 0)
            project_v(0, 0, 0)
            scores(0, 0, 0, 1)
            project_v(0, 0, 1)
            scores(0, 0, 1, 0)
            project_v(0, 0, 2)
            project_v(0, 0, 3)
            over_quads(pe, quad)

        @block.scalar
        def _(act):
            def keep_xT_hi(j, p, c):
                act.wait_ge(xT_loaded, 16 * (2 * j + p) + 16)
                nc.scalar.activation(xT_hi[p][:, c, :], xT_raw[:, c, :], ACT.Copy).then_inc(xT_hi_done, 1)

            def keep_w_hi(part):
                cols, factor = W_PARTS[part]
                act.wait_ge(w_loaded[cols.start // HIDDEN], 16)
                nc.scalar.activation(w_hi[:, :, cols], w_raw[:, :, cols], ACT.Copy, scale=factor)\
                    .then_inc(w_hi_done, 1)

            def keep_qk(j, p, k):
                act.wait_ge(qk_psum, QK * (2 * j + p) + k + 1)
                nc.scalar.activation(qkT[p][:, k, :], proj_bank[k % 2][:, :], ACT.Copy)\
                    .then_inc(qk_done, 1)

            def exp_trio(j, p, b, trio):
                act.wait_ge(neg_a_done, 4 * (QUAD * (2 * j + p) + b) + trio + 1)
                for u in range(CHUNKS * trio, CHUNKS * (trio + 1)):
                    last = nc.scalar.activation(probs[b % 2][:, u, :], neg_a[b % 2][:, u, :], ACT.Exp,
                                                bias=neg_max[b % 2][:, u:u + 1], scale=-1.0,
                                                accum_out=row_sum[b % 2][:, u:u + 1])
                last.then_inc(exp_done, 1)

            def keep_pT(j, p, b, trio):
                act.wait_ge(pT_psum, 4 * (QUAD * (2 * j + p) + b) + trio + 1)
                nc.scalar.activation(pT[:, CHUNKS * trio:CHUNKS * (trio + 1), :],
                                     pT_bank[trio % 2][:, 0:HIDDEN].rearrange("p (c n) -> p c n", c=CHUNKS),
                                     ACT.Copy).then_inc(pT_done, 1)

            def keep_oT_hi(j, p, b):
                act.wait_ge(oT_psum, QUAD * (2 * j + p) + b + 1)
                nc.scalar.activation(oT_hi[:, :, :],
                                     oT_bank[:, 0:HIDDEN].rearrange("p (c n) -> p c n", c=CHUNKS),
                                     ACT.Copy).then_inc(oT_hi_done, 1)

            def graph(j, p, b, has_next, has_after):
                nxt, aft = ahead(j, p, 1), ahead(j, p, 2)

                def beside_cover(step):
                    if has_next and b < 2:
                        keep_qk(*nxt, 3 * b + step)
                    elif has_after and b == 2:
                        keep_xT_hi(*aft, step)

                beside_cover(0)
                for trio in range(4):
                    keep_pT(j, p, b, trio)
                if b + 1 < QUAD or has_next:
                    exp_trio(*later(j, p, b, 1), 2)
                beside_cover(1)
                keep_oT_hi(j, p, b)
                if b + 1 < QUAD or has_next:
                    exp_trio(*later(j, p, b, 1), 3)
                if b + 2 < QUAD or has_next:
                    exp_trio(*later(j, p, b, 2), 0)
                beside_cover(2)
                if b + 2 < QUAD or has_next:
                    exp_trio(*later(j, p, b, 2), 1)

            def quad(j, p, has_next, has_after):
                for b in range(QUAD):
                    graph(j, p, b, has_next, has_after)

            for c in range(CHUNKS):
                keep_xT_hi(0, 0, c)
            for part in range(4):
                keep_w_hi(part)
            for k in range(QK):
                keep_qk(0, 0, k)
                if k < 2:
                    keep_w_hi(4 + k)
                if k >= CHUNKS:
                    keep_xT_hi(0, 1, k - CHUNKS)
            for trio in range(4):
                exp_trio(0, 0, 0, trio)
            for trio in range(2):
                exp_trio(0, 0, 1, trio)
            over_quads(act, quad)

        @block.vector
        def _(dve):
            def wait_alone(semaphore, count):
                dve.compute_val(count)
                dve.wait_ge(b_loaded, 32)
                dve.wait_ge(semaphore, count)

            def keep_xT_lo(j, p, c):
                dve.wait_ge(xT_hi_done, CHUNKS * (2 * j + p) + c + 1)
                nc.vector.tensor_tensor(xT_lo[p][:, c, :], xT_raw[:, c, :],
                                        xT_hi[p][:, c, :].bitcast(f32), ALU.subtract).then_inc(xT_lo_done, 1)

            def keep_w_lo(part):
                dve.wait_ge(w_hi_done, part + 1)
                cols, factor = W_PARTS[part]
                nc.vector.scalar_tensor_tensor(out=w_lo[:, :, cols], in0=w_raw[:, :, cols],
                                               scalar=factor,
                                               in1=w_hi[:, :, cols].bitcast(f32), op0=ALU.mult,
                                               op1=ALU.subtract).then_inc(w_lo_done, 1)

            def keep_v(j, p, b):
                dve.wait_ge(v_psum, QUAD * (2 * j + p) + b + 1)
                nc.vector.tensor_tensor(v_sb[p][:, b, :], proj_bank[b % 2][:, 0:HIDDEN], bv_sb[:, :],
                                        ALU.add).then_inc(v_done, 1)

            def bias_trio(j, p, b, trio):
                if b == 0 and trio == 0:
                    dve.wait_ge(adj_loaded[p], 16 * (j + 1))
                wait_alone(scores_psum, 4 * (QUAD * (2 * j + p) + b) + trio + 1)
                for c in range(CHUNKS):
                    u = CHUNKS * trio + c
                    last = nc.vector.tensor_tensor_reduce(
                        out=neg_a[b % 2][:, u, :], in0=score_bank[trio % 2][:, c * N:(c + 1) * N],
                        in1=adj_sb[p][:, b, :], scale=-1.0, scalar=BIG, op0=ALU.add, op1=ALU.min,
                        accum_out=neg_max[b % 2][:, u:u + 1])
                last.then_inc(neg_a_done, 1)

            def mask_sum(j, p, b, half):
                u = slice(HALF * half, HALF * (half + 1))
                dve.wait_ge(fold_done, 2 * (QUAD * (2 * j + p) + b) + half + 1)
                nc.vector.tensor_reduce(neg_sum[:, u], fold[:, u, :], AX.X, ALU.add).then_inc(mask_steps, 1)

            def mask_reciprocal(j, p, b, half):
                u = slice(HALF * half, HALF * (half + 1))
                dve.wait_ge(exp_done, 4 * (QUAD * (2 * j + p) + b) + 2 * half + 2)
                nc.vector.reciprocal(inv_sum[:, u], row_sum[b % 2][:, u]).then_inc(mask_steps, 1)

            def mask_live(j, p, b, half):
                u = slice(HALF * half, HALF * (half + 1))
                dve.wait_ge(mask_steps, MASK_STEPS * (QUAD * (2 * j + p) + b) + 3 * half + 1)
                nc.vector.tensor_tensor(live[:, u], neg_max[b % 2][:, u], neg_sum[:, u],
                                        ALU.logical_or).then_inc(mask_steps, 1)

            def mask_scale(j, p, b, half):
                u = slice(HALF * half, HALF * (half + 1))
                dve.wait_ge(mask_steps, MASK_STEPS * (QUAD * (2 * j + p) + b) + 3 * half + 3)
                nc.vector.tensor_tensor(row_scale[:, u], live[:, u], inv_sum[:, u], ALU.mult)\
                    .then_inc(scale_done, 1)

            def mask_half(j, p, b, half):
                for step in (mask_sum, mask_reciprocal, mask_live, mask_scale):
                    step(j, p, b, half)

            def keep_oT_lo(j, p, b):
                dve.wait_ge(oT_hi_done, QUAD * (2 * j + p) + b + 1)
                nc.vector.tensor_tensor(oT_lo[:, :, :],
                                        oT_bank[:, 0:HIDDEN].rearrange("p (c n) -> p c n", c=CHUNKS),
                                        oT_hi[:, :, :].bitcast(f32), ALU.subtract).then_inc(oT_lo_done, 1)

            def residual(j, p, b):
                dve.wait_ge(xb_done, QUAD * (2 * j + p) + b + 1)
                dve.wait_ge(y_psum, QUAD * (2 * j + p) + b + 1)
                nc.vector.tensor_tensor(y_sb[:, :], y_bank[:, 0:HIDDEN], x_sb[p][:, b, :], ALU.add)\
                    .then_inc(ln_steps, 1)

            def statistics(j, p, b):
                dve.wait_ge(ln_steps, LN_STEPS * (QUAD * (2 * j + p) + b) + 1)
                nc.vector.bn_stats(stats[:, :], y_sb[:, :]).then_inc(ln_steps, 1)

            def mean_variance(j, p, b):
                wait_alone(ln_steps, LN_STEPS * (QUAD * (2 * j + p) + b) + 2)
                nc.vector.bn_aggr(mean_var[:, :], stats[:, :]).then_inc(ln_steps, 1)

            def add_eps(j, p, b):
                dve.wait_ge(ln_steps, LN_STEPS * (QUAD * (2 * j + p) + b) + 3)
                nc.vector.tensor_scalar(var_eps[:, :], mean_var[:, 1:2], EPS, None, ALU.add)\
                    .then_inc(ln_steps, 1)

            def normalise(j, p, b):
                t = QUAD * (2 * j + p) + b
                dve.wait_ge(inv_std_done, t + 1)
                dve.wait_ge(out_stored[b], 16 * (2 * j + p) + 16)
                nc.vector.tensor_scalar(out_sb[:, b, :], y_sb[:, :], mean_var[:, 0:1], inv_std[:, 0:1],
                                        ALU.subtract, ALU.mult).then_inc(out_done, 1)

            def graph(j, p, b, has_next, has_after):
                nxt, aft = ahead(j, p, 1), ahead(j, p, 2)
                more = b + 1 < QUAD or has_next
                more2 = b + 2 < QUAD or has_next
                if has_next and b >= 2:
                    keep_v(*nxt, 2 * (b - 2))
                keep_oT_lo(j, p, b)
                if more2:
                    bias_trio(*later(j, p, b, 2), 0)
                    bias_trio(*later(j, p, b, 2), 1)
                if more:
                    mask_half(*later(j, p, b, 1), 1)
                if has_after and b >= 2:
                    keep_xT_lo(*aft, 2 * (b - 2))
                if has_next and b >= 2:
                    keep_v(*nxt, 2 * (b - 2) + 1)
                residual(j, p, b)
                statistics(j, p, b)
                mean_variance(j, p, b)
                add_eps(j, p, b)
                if more2:
                    bias_trio(*later(j, p, b, 2), 2)
                    bias_trio(*later(j, p, b, 2), 3)
                    mask_half(*later(j, p, b, 2), 0)
                normalise(j, p, b)
                if has_after and b == 2:
                    keep_xT_lo(*aft, 1)

            def quad(j, p, has_next, has_after):
                for b in range(QUAD):
                    graph(j, p, b, has_next, has_after)

            for c in range(CHUNKS):
                keep_xT_lo(0, 0, c)
            for part in range(len(W_PARTS)):
                keep_w_lo(part)
            for c in range(CHUNKS):
                keep_xT_lo(0, 1, c)
            dve.wait_ge(b_loaded, 32)
            bias_trio(0, 0, 0, 0)
            bias_trio(0, 0, 0, 1)
            keep_v(0, 0, 0)
            bias_trio(0, 0, 0, 2)
            bias_trio(0, 0, 0, 3)
            keep_v(0, 0, 1)
            mask_half(0, 0, 0, 0)
            bias_trio(0, 0, 1, 0)
            bias_trio(0, 0, 1, 1)
            keep_v(0, 0, 2)
            mask_half(0, 0, 0, 1)
            keep_v(0, 0, 3)
            bias_trio(0, 0, 1, 2)
            bias_trio(0, 0, 1, 3)
            mask_half(0, 0, 1, 0)
            over_quads(dve, quad)

        @block.gpsimd
        def _(pool):
            def add_bo(j, p, b):
                if b == 0:
                    pool.wait_ge(x_loaded[p], 16 * (j + 1))
                nc.gpsimd.tensor_tensor(x_sb[p][:, b, :], x_sb[p][:, b, :], bo_sb[:, :], ALU.add)\
                    .then_inc(xb_done, 1)

            def fold_half(j, p, b, half):
                u = slice(HALF * half, HALF * (half + 1))
                pool.wait_ge(neg_a_done, 4 * (QUAD * (2 * j + p) + b) + 2 * half + 2)
                nc.gpsimd.tensor_tensor(fold[:, u, :], neg_a[b % 2][:, u, 0:N // 2],
                                        neg_a[b % 2][:, u, N // 2:N], ALU.add).then_inc(fold_done, 1)

            def scale_half(j, p, b, half):
                u = slice(HALF * half, HALF * (half + 1))
                pool.wait_ge(scale_done, 2 * (QUAD * (2 * j + p) + b) + half + 1)
                nc.gpsimd.tensor_tensor(probs[b % 2][:, u, :], probs[b % 2][:, u, :],
                                        row_scale[:, u].unsqueeze(2).broadcast_to([P, HALF, N]),
                                        ALU.mult).then_inc(probs_done, 1)

            def inverse_std(j, p, b):
                pool.wait_ge(ln_steps, LN_STEPS * (QUAD * (2 * j + p) + b) + 4)
                nc.gpsimd.tensor_tensor(inv_std[:, :], var_eps[:, :], minus_half[:, :], ALU.pow)\
                    .then_inc(inv_std_done, 1)

            def quad(j, p, has_next, has_after):
                for b in range(QUAD):
                    more = b + 1 < QUAD or has_next
                    if more:
                        scale_half(*later(j, p, b, 1), 0)
                        fold_half(*later(j, p, b, 1), 1)
                    if b + 2 < QUAD or has_next:
                        add_bo(*later(j, p, b, 2))
                    if more:
                        scale_half(*later(j, p, b, 1), 1)
                    if b + 2 < QUAD or has_next:
                        fold_half(*later(j, p, b, 2), 0)
                    inverse_std(j, p, b)

            nc.gpsimd.memset(ident[:, :], 0.0).then_inc(ident_steps, 1)
            pool.wait_ge(ident_steps, 1)
            nc.gpsimd.affine_select(out=ident[:, :], in_=ident[:, :], compare_op=ALU.not_equal, fill=1.0,
                                    base=0, pattern=[[-1, P]], channel_multiplier=1).then_inc(ident_steps, 1)
            nc.gpsimd.memset(minus_half[:, :], -0.5).then_inc(ident_steps, 1)
            pool.wait_ge(ident_steps, 3)
            pool.wait_ge(b_loaded, 32)
            for b in range(2):
                add_bo(0, 0, b)
            for half in range(2):
                fold_half(0, 0, 0, half)
            for half in range(2):
                scale_half(0, 0, 0, half)
            fold_half(0, 0, 1, 0)
            over_quads(pool, quad)


_OUT = "out_dram"


def kernel(x, adj, L0_gnn_Wq, L0_gnn_Wk, L0_gnn_Wv, L0_gnn_bv, L0_gnn_Wo, L0_gnn_bo):
    import numpy as np
    import concourse.bacc as bacc
    from concourse.bass_utils import run_bass_kernel_spmd

    x_quads = np.asarray(x).reshape(QUADS, QUAD, N, CHUNKS, P)
    arrays = {
        "x_dram": np.ascontiguousarray(x),
        "xT_dram": np.ascontiguousarray(x_quads.transpose(0, 4, 3, 1, 2)).reshape(QUADS, P, CHUNKS, TOK),
        "adj_dram": np.ascontiguousarray(adj),
        "wq_t_dram": np.ascontiguousarray(np.asarray(L0_gnn_Wq).T),
        "wk_t_dram": np.ascontiguousarray(np.asarray(L0_gnn_Wk).T),
        "wv_t_dram": np.ascontiguousarray(np.asarray(L0_gnn_Wv).T),
        "wo_t_dram": np.ascontiguousarray(np.asarray(L0_gnn_Wo).T),
        "bv_dram": np.ascontiguousarray(L0_gnn_bv), "bo_dram": np.ascontiguousarray(L0_gnn_bo),
    }
    nc = bacc.Bacc("TRN2", target_bir_lowering=False, num_devices=1)
    args = [nc.dram_tensor(name, a.shape, mybir.dt.from_np(a.dtype), kind="ExternalInput").ap()
            for name, a in arrays.items()]
    out = nc.dram_tensor(_OUT, (BATCH, N, HIDDEN), mybir.dt.float32, kind="ExternalOutput").ap()
    attention_kernel(nc, *args, out)
    r = run_bass_kernel_spmd(nc, [arrays], core_ids=[0])
    return r.results[0][_OUT]
```
